# Optimizing a Trainium2 kernel written in Bass

```python
import numpy as np
import jax
import jax.numpy as jnp

def _softmax(x, axis=-1):
    return jax.nn.softmax(x, axis=axis)

def _gelu(x):
    return jax.nn.gelu(x, approximate=True)

def _silu(x):
    return jax.nn.silu(x)

def _sigmoid(x):
    return jax.nn.sigmoid(x)

def _layernorm(x, axis=-1, eps=1e-05):
    m = jnp.mean(x, axis=axis, keepdims=True)
    v = jnp.var(x, axis=axis, keepdims=True)
    return (x - m) / jnp.sqrt(v + eps)

def _scatter_add(tgt, idx, src, axis=0):
    return tgt.at[idx].add(src)

def _segment_sum(src, seg, n):
    return jax.ops.segment_sum(src, seg, n)
kernel_name = 'mk_adaln_ffn_d1_seqx_r8_4db4c5'

def setup_inputs(seed: int=0):
    np.random.seed(seed)
    _w = jnp.asarray

    def _rec_inputs():
        import jax
        import jax.numpy as jnp
        _rk = jax.random.key(seed)
        x = -7.109e-05 + 0.9999 * jax.random.normal(jax.random.fold_in(_rk, 1), (64, 32, 512), jnp.float32)
        _lenS = 32 - jax.random.randint(jax.random.fold_in(_rk, 7), (64,), 0, max(1, 32 // 4) + 1, jnp.int32)
        _lenS2 = 32 - jax.random.randint(jax.random.fold_in(_rk, 8), (64,), 0, max(1, 32 // 4) + 1, jnp.int32)
        itok_B_0_15 = jax.random.randint(jax.random.fold_in(_rk, 11), (64,), 0, 16, jnp.int32)
        return (x, itok_B_0_15)
    x, itok_B_0_15 = _rec_inputs()

    def _L0_cond_setup():
        import jax, jax.numpy as jnp
        import numpy as np
        B, C, T = (64, 32, 512)
        S, D = (16, 32)
        key = jax.random.key(seed)
        k1, k2, k3 = jax.random.split(key, 3)
        x = jax.random.normal(k1, (B, C, T), dtype=jnp.float32)
        condition = jax.random.randint(k2, (B,), 0, S, dtype=jnp.int64)
        bound = float(np.sqrt(6.0 / C))
        weights = jax.random.uniform(k3, (S, C, D), dtype=jnp.float32, minval=-bound, maxval=bound)
        return {'x': x, 'condition': condition, 'weights': weights}
    _L0_cond_all = _L0_cond_setup()
    _L0_cond_in = {k: v for k, v in _L0_cond_all.items() if k in ('weights',)}
    del _L0_cond_all

    def _L0_ffn_setup():
        import jax, jax.numpy as jnp
        import numpy as np
        BATCH, TOK, DIM, OUT = (4, 256, 512, 512)
        E, R, TOP_K = (8, 16, 2)
        SCALING = 16.0 / R
        key = jax.random.key(seed)
        ks = jax.random.split(key, 6)
        return {'x': jax.random.normal(ks[0], (BATCH, TOK, DIM), dtype=jnp.float32), 'W_base': jax.random.normal(ks[1], (OUT, DIM), dtype=jnp.float32) / np.sqrt(DIM), 'b_base': jax.random.normal(ks[2], (OUT,), dtype=jnp.float32) * 0.01, 'W_gate': jax.random.normal(ks[3], (E, DIM), dtype=jnp.float32) * 0.01, 'A': jax.random.normal(ks[4], (E, R, DIM), dtype=jnp.float32) / np.sqrt(DIM), 'B': jax.random.normal(ks[5], (OUT, OUT // OUT * R * 0 + R), dtype=jnp.float32)[None].repeat(E, 0) * 0.0 + jax.random.normal(ks[5], (E, OUT, R), dtype=jnp.float32) * 0.02}
    _L0_ffn_all = _L0_ffn_setup()
    _L0_ffn_in = {k: v for k, v in _L0_ffn_all.items() if k in ('W_base', 'b_base', 'W_gate', 'A', 'B')}
    del _L0_ffn_all
    return {'x': x, 'itok_B_0_15': itok_B_0_15, 'L0_cond_weights': _L0_cond_in['weights'], 'L0_ffn_W_base': _L0_ffn_in['W_base'], 'L0_ffn_b_base': _L0_ffn_in['b_base'], 'L0_ffn_W_gate': _L0_ffn_in['W_gate'], 'L0_ffn_A': _L0_ffn_in['A'], 'L0_ffn_B': _L0_ffn_in['B']}

def reference(x, itok_B_0_15, L0_cond_weights, L0_ffn_W_base, L0_ffn_b_base, L0_ffn_W_gate, L0_ffn_A, L0_ffn_B):
    import jax
    import jax.numpy as jnp

    def _L0_cond_ref(x, condition, weights):
        import jax, jax.numpy as jnp
        import numpy as np
        B, C, T = (64, 32, 512)
        S, D = (16, 32)
        W = weights[condition]
        return jnp.einsum('bct,bcd->bdt', x, W)

    def _L0_ffn_ref(x, W_base, b_base, W_gate, A, B):
        import jax, jax.numpy as jnp
        import numpy as np
        BATCH, TOK, DIM, OUT = (4, 256, 512, 512)
        E, R, TOP_K = (8, 16, 2)
        SCALING = 16.0 / R
        result = jnp.einsum('bnd,od->bno', x, W_base) + b_base
        logits = jnp.einsum('bnd,ed->bne', x, W_gate)
        probs = jax.nn.softmax(logits.astype(jnp.float32), axis=-1)
        top_p, top_i = jax.lax.top_k(probs, TOP_K)
        top_p = top_p / jnp.sum(top_p, axis=-1, keepdims=True)
        top_p = top_p.astype(x.dtype)
        route_w = jnp.sum(jax.nn.one_hot(top_i, E, dtype=x.dtype) * top_p[..., None], axis=-2)
        h = jnp.einsum('bnd,erd->bner', x, A)
        hw = h * route_w[..., None]
        delta = jnp.einsum('bner,eor->bno', hw, B)
        return result + delta * SCALING
    x = x + _L0_ffn_ref(_L0_cond_ref(x, itok_B_0_15, L0_cond_weights), L0_ffn_W_base, L0_ffn_b_base, L0_ffn_W_gate, L0_ffn_A, L0_ffn_B)
    return x

_drawn_inputs = setup_inputs


def setup_inputs(seed=0):
    import zlib

    import numpy as np

    out = dict(_drawn_inputs(seed))
    spreads = {}
    factors = {'L0_ffn_b_base': 8.0}
    for name, (base, spread) in spreads.items():
        noise = np.random.default_rng([zlib.crc32(name.encode()), seed]).standard_normal(out[name].shape)
        drawn = base * np.exp(spread * noise) if base else spread * noise
        out[name] = jnp.asarray(drawn.astype(out[name].dtype))
    for name, factor in factors.items():
        out[name] = (out[name] * factor).astype(out[name].dtype)
    return out
```

```python
import concourse.bass as bass
from concourse import mybir
from contextlib import ExitStack


def adaln_ffn_kernel(
    nc: bass.Bass,
    x: bass.AP,
    cond: bass.AP,
    cond_w: bass.AP,
    w_all: bass.AP,
    b_lora: bass.AP,
    bias: bass.AP,
    out: bass.AP,
):
    f32 = mybir.dt.float32
    f32r = mybir.dt.float32r
    i32 = mybir.dt.int32
    u32 = mybir.dt.uint32
    ALU = mybir.AluOpType
    ACT = mybir.ActivationFunctionType

    P = 128
    BATCHES, C, D = x.shape
    Q = P // C
    TILES = BATCHES // Q
    CHUNKS = D // P
    RANKS = b_lora.shape[0]
    E = w_all.shape[1] - D - RANKS
    R = RANKS // E
    OUT = D
    SIDE = RANKS + E
    ALL = OUT + SIDE
    PAIRS = TILES // 2

    x_tiles = x.rearrange("(t q) c n -> t (q c) n", q=Q)
    out_tiles = out.rearrange("(t q) c n -> t (q c) n", q=Q)
    w_chunks = w_all.rearrange("(c p) n -> c p n", p=P)

    ctx = ExitStack()
    with ctx:
        def sb(name, shape, dt=f32):
            return ctx.enter_context(nc.sbuf_tensor(name, shape, dt))

        def ps(name):
            return ctx.enter_context(nc.psum_tensor(name, [P, 512], f32))

        def sem(name):
            return ctx.enter_context(nc.semaphore(name))

        x_all = sb("x_all", [P, TILES * D])
        xb_all = sb("xb_all", [P, TILES * D])
        w_raw = sb("w_raw", [P, CHUNKS, ALL])
        w_hi = sb("w_hi", [P, CHUNKS, ALL], f32r)
        w_lo = sb("w_lo", [P, CHUNKS, ALL], f32r)
        b_raw = sb("b_raw", [P, OUT])
        b_hi = sb("b_hi", [P, OUT], f32r)
        b_lo = sb("b_lo", [P, OUT], f32r)
        bias_sb = sb("bias_sb", [P, OUT])
        ident = sb("ident", [P, P])
        diag_mask = sb("diag_mask", [P, Q, C])
        channel = sb("channel", [P, 1], i32)
        expert_ids = sb("expert_ids", [P, E])
        cond_sb = sb("cond_sb", [P, TILES], i32)
        row_ids = sb("row_ids", [P, TILES], i32)
        row_now = [sb(f"row_now{i}", [P, 1], i32) for i in range(2)]
        mixw = [sb(f"mixw{i}", [P, C]) for i in range(2)]
        mixw_split = sb("mixw_split", [P, 2, C])
        mix = [sb(f"mix{i}", [P, 2, Q * C], f32r) for i in range(2)]
        x_hi = [sb(f"x_hi{i}", [P, D], f32r) for i in range(2)]
        x_lo = [sb(f"x_lo{i}", [P, D], f32r) for i in range(2)]
        y_hi = [sb(f"y_hi{i}", [P, D], f32r) for i in range(2)]
        y_lo = [sb(f"y_lo{i}", [P, D], f32r) for i in range(2)]
        hw = [sb(f"hw{i}", [P, RANKS]) for i in range(2)]
        hwT_hi = [sb(f"hwT_hi{i}", [P, P], f32r) for i in range(2)]
        hwT_lo = [sb(f"hwT_lo{i}", [P, P], f32r) for i in range(2)]
        top = sb("top", [P, 8])
        top_ids = sb("top_ids", [P, 8], u32)
        one_hot = sb("one_hot", [P, 2, E])
        second = sb("second", [P, 1])
        total = sb("total", [P, 1])
        weight = sb("weight", [P, 1])
        route = sb("route", [P, E])

        y_ps = [ps(f"y_ps{i}") for i in range(2)]
        base_ps = [ps(f"base_ps{i}") for i in range(2)]
        side_ps = [ps(f"side_ps{i}") for i in range(2)]
        hwT_ps = [ps(f"hwT_ps{i}") for i in range(2)]

        x_landed = [sem(f"x_landed{i}") for i in range(2)]
        cond_landed = sem("cond_landed")
        w_landed = [sem(f"w_landed{c}") for c in range(CHUNKS)]
        b_landed = sem("b_landed")
        bias_landed = sem("bias_landed")
        mixw_landed = [sem(f"mixw_landed{i}") for i in range(2)]
        channel_ready = sem("channel_ready")
        cleared = sem("cleared")
        mask_ready = sem("mask_ready")
        experts_ready = sem("experts_ready")
        ident_ready = sem("ident_ready")
        rows_ready = sem("rows_ready")
        row_staged = sem("row_staged")
        mixw_hi_ready = sem("mixw_hi_ready")
        mixw_lo_ready = sem("mixw_lo_ready")
        mix_ready = sem("mix_ready")
        x_hi_ready = sem("x_hi_ready")
        x_lo_ready = sem("x_lo_ready")
        xb_ready = sem("xb_ready")
        w_hi_ready = sem("w_hi_ready")
        w_lo_ready = sem("w_lo_ready")
        b_hi_ready = sem("b_hi_ready")
        b_lo_ready = sem("b_lo_ready")
        y_done = sem("y_done")
        y_hi_ready = sem("y_hi_ready")
        y_lo_ready = sem("y_lo_ready")
        main_done = sem("main_done")
        top_ready = sem("top_ready")
        ids_ready = sem("ids_ready")
        one_hot_ready = sem("one_hot_ready")
        second_ready = sem("second_ready")
        total_ready = sem("total_ready")
        weight_ready = sem("weight_ready")
        hw_ready = sem("hw_ready")
        hwT_done = sem("hwT_done")
        hwT_hi_ready = sem("hwT_hi_ready")
        hwT_lo_ready = sem("hwT_lo_ready")
        base_done = sem("base_done")
        result_ready = sem("result_ready")
        stored = sem("stored")

        def cols(buf, t):
            return buf[:, bass.ds(t * D, D)]

        def over_tiles(eng, step):
            for slot in range(2):
                step(slot, slot, 0)
            with eng.Fori(1, PAIRS - 1) as pair:
                for slot in range(2):
                    step(pair * 2 + slot, slot, pair)
            for slot in range(2):
                step(TILES - 2 + slot, slot, PAIRS - 1)

        def known(t):
            return isinstance(t, int)

        def held(eng, value):
            return value if known(value) else eng.to_reg(value)

        def at_least(t, n):
            return t >= n if known(t) else True

        def exists(t, ahead):
            return t + ahead < TILES if known(t) else True

        block = ctx.enter_context(nc.Block())

        @block.sync
        def _(sp):
            for q in range(Q):
                sp.dma_start(cond_sb[q * C:(q + 1) * C, :],
                             cond[q:q + 1, :].to_broadcast([C, TILES])).then_inc(cond_landed, 16)

            def load_x(t, slot, pair):
                if at_least(t, 2):
                    sp.wait_ge(x_landed[slot], pair * 16)
                sp.dma_start(cols(x_all, t), x_tiles[t, :, :]).then_inc(x_landed[slot], 16)
            over_tiles(sp, load_x)

            def store(t, slot, pair):
                sp.wait_ge(result_ready, t + 1)
                sp.dma_start(out_tiles[t, :, :], cols(xb_all, t)).then_inc(stored, 16)
            over_tiles(sp, store)
            sp.wait_ge(stored, 16 * TILES)

        @block.gpsimd
        def _(pool):
            for q in range(Q):
                last = pool.iota(channel[q * C:(q + 1) * C, :], [[0, 1]], base=0, channel_multiplier=1)
            last.then_inc(channel_ready, 1)

            def gather(t, slot):
                if at_least(t, 2):
                    pool.wait_ge(mix_ready, t - 1)
                count = held(pool, t + 1)
                pool.tensor_copy(row_now[slot][:, :], row_ids[:, bass.ds(t, 1)]).then_inc(row_staged, 1)
                pool.wait_ge(rows_ready, 1)
                pool.wait_ge(row_staged, count)
                pool.indirect_dma_start(mixw[slot][:, :], None, cond_w,
                                        bass.IndirectOffsetOnAxis(row_now[slot][:, 0:1], 0))\
                    .then_inc(mixw_landed[slot], 16)

            pool.wait_ge(rows_ready, 1)
            gather(0, 0)
            gather(1, 1)
            pool.memset(diag_mask[:, :, :], 0.0).then_inc(cleared, 1)
            pool.memset(ident[:, :], 0.0).then_inc(cleared, 1)
            pool.wait_ge(cleared, 2)
            for q in range(Q):
                last = pool.memset(diag_mask[q * C:(q + 1) * C, q, :], 1.0)
            last.then_inc(mask_ready, 1)
            pool.wait_ge(mask_ready, 1)
            pool.affine_select(out=ident[:, :], in_=ident[:, :], compare_op=ALU.not_equal, fill=1.0,
                               base=0, pattern=[[-1, P]], channel_multiplier=1).then_inc(ident_ready, 1)
            pool.wait_ge(ident_ready, 1)
            pool.iota(expert_ids[:, :], [[1, E]], base=0, channel_multiplier=0,
                      allow_small_or_imprecise_dtypes=True).then_inc(experts_ready, 1)

            def prepare(t, slot, pair):
                pool.wait_ge(x_hi_ready, t + 1)
                pool.tensor_tensor(x_lo[slot][:, :], cols(x_all, t), x_hi[slot][:, :].bitcast(f32),
                                   ALU.subtract).then_inc(x_lo_ready, 1)
                if exists(t, 2):
                    gather(t + 2, slot)
                if not at_least(t, 1):
                    pool.wait_ge(bias_landed, 16)
                pool.tensor_tensor(cols(xb_all, t), cols(x_all, t), bias_sb[:, :], ALU.add)\
                    .then_inc(xb_ready, 1)
            over_tiles(pool, prepare)

        @block.scalar
        def _(act):
            for c in range(CHUNKS):
                act.dma_start(w_raw[:, c, :], w_chunks[c, :, :]).then_inc(w_landed[c], 16)
            act.dma_start(bias_sb[:, :], bias.to_broadcast([P, OUT])).then_inc(bias_landed, 16)
            act.dma_start(b_raw[:, :], b_lora).then_inc(b_landed, 16)

            def split_x(t, slot, pair):
                act.wait_ge(x_landed[slot], pair * 16 + 16)
                if at_least(t, 2):
                    act.wait_ge(y_done, t - 1)
                act.activation(x_hi[slot][:, :], cols(x_all, t), ACT.Copy).then_inc(x_hi_ready, 1)

            def split_w(c):
                act.wait_ge(w_landed[c], 16)
                act.activation(w_hi[:, c, :], w_raw[:, c, :], ACT.Copy).then_inc(w_hi_ready, 1)

            def split_y(t, slot):
                act.wait_ge(y_done, t + 1)
                if at_least(t, 2):
                    act.wait_ge(main_done, t - 1)
                act.activation(y_hi[slot][:, :], y_ps[slot][:, :], ACT.Copy).then_inc(y_hi_ready, 1)

            def exp_second(t):
                act.wait_ge(top_ready, t + 1)
                act.activation(second[:, :], top[:, 0:1], ACT.Exp, bias=top[:, 1:2], scale=-1.0)\
                    .then_inc(second_ready, 1)

            def split_hwT(t, slot):
                act.wait_ge(hwT_done, t + 1)
                if at_least(t, 2):
                    act.wait_ge(base_done, t - 1)
                act.activation(hwT_hi[slot][:, :], hwT_ps[slot][:, 0:P], ACT.Copy)\
                    .then_inc(hwT_hi_ready, 1)

            split_x(0, 0, 0)
            split_x(1, 1, 0)
            for c in range(CHUNKS):
                split_w(c)
            split_y(0, 0)
            act.wait_ge(b_landed, 16)
            act.activation(b_hi[:, :], b_raw[:, :], ACT.Copy).then_inc(b_hi_ready, 1)

            def step(t, slot, pair):
                if at_least(t, 1):
                    exp_second(t - 1)
                if exists(t, 1):
                    split_y(t + 1, 1 - slot)
                if exists(t, 2):
                    split_x(t + 2, slot, pair + 1)
                if at_least(t, 1):
                    split_hwT(t - 1, 1 - slot)
            over_tiles(act, step)
            exp_second(TILES - 1)
            split_hwT(TILES - 1, 1)

        @block.vector
        def _(dve):
            dve.wait_ge(cond_landed, 16 * Q)
            dve.wait_ge(channel_ready, 1)
            dve.scalar_tensor_tensor(out=row_ids[:, :], in0=cond_sb[:, :], scalar=float(C),
                                     in1=channel[:, 0:1].to_broadcast([P, TILES]),
                                     op0=ALU.mult, op1=ALU.add).then_inc(rows_ready, 1)

            def select(t, slot, pair):
                dve.wait_ge(mixw_landed[slot], pair * 16 + 16)
                if at_least(t, 1):
                    dve.wait_ge(mix_ready, t)
                dve.tensor_copy(mixw_split[:, 0, :].bitcast(f32r), mixw[slot][:, :])\
                    .then_inc(mixw_hi_ready, 1)
                dve.wait_ge(mixw_hi_ready, t + 1)
                dve.tensor_tensor(mixw_split[:, 1, :], mixw[slot][:, :], mixw_split[:, 0, :],
                                  ALU.subtract).then_inc(mixw_lo_ready, 1)
                dve.wait_ge(mixw_lo_ready, t + 1)
                dve.tensor_tensor(mix[slot][:, :, :].rearrange("p s (q d) -> p s q d", q=Q),
                                  mixw_split[:, :, :].unsqueeze(2).to_broadcast([P, 2, Q, C]),
                                  diag_mask[:, :, :].unsqueeze(1).to_broadcast([P, 2, Q, C]),
                                  ALU.mult).then_inc(mix_ready, 1)

            def low_w(c):
                dve.wait_ge(w_hi_ready, c + 1)
                dve.tensor_tensor(w_lo[:, c, :], w_raw[:, c, :], w_hi[:, c, :].bitcast(f32),
                                  ALU.subtract).then_inc(w_lo_ready, 1)

            def low_y(t, slot):
                dve.wait_ge(y_hi_ready, t + 1)
                dve.tensor_tensor(y_lo[slot][:, :], y_ps[slot][:, :], y_hi[slot][:, :].bitcast(f32),
                                  ALU.subtract).then_inc(y_lo_ready, 1)

            def route_tile(t, slot):
                logits = side_ps[slot][:, RANKS:SIDE]
                count = held(dve, t + 1)
                dve.wait_ge(experts_ready, 1)
                dve.wait_ge(main_done, count)
                dve.max(top[:, :], logits).then_inc(top_ready, 1)
                dve.wait_ge(experts_ready, 1)
                dve.wait_ge(top_ready, count)
                dve.max_index(top_ids[:, :], top[:, :], logits).then_inc(ids_ready, 1)
                dve.wait_ge(ids_ready, t + 1)
                dve.tensor_tensor(one_hot[:, :, :],
                                  expert_ids[:, :].unsqueeze(1).to_broadcast([P, 2, E]),
                                  top_ids[:, 0:2].unsqueeze(2).to_broadcast([P, 2, E]),
                                  ALU.is_equal).then_inc(one_hot_ready, 1)
                dve.wait_ge(second_ready, t + 1)
                dve.tensor_scalar(total[:, :], second[:, :], 1.0, None, ALU.add).then_inc(total_ready, 1)
                dve.wait_ge(one_hot_ready, t + 1)
                if at_least(t, 1):
                    dve.wait_ge(hw_ready, t)
                dve.scalar_tensor_tensor(out=route[:, :], in0=one_hot[:, 1, :], scalar=second[:, 0:1],
                                         in1=one_hot[:, 0, :], op0=ALU.mult, op1=ALU.add)
                dve.wait_ge(total_ready, t + 1)
                dve.reciprocal(weight[:, :], total[:, :]).then_inc(weight_ready, 1)
                dve.wait_ge(weight_ready, t + 1)
                dve.scalar_tensor_tensor(out=hw[slot][:, :].rearrange("p (e r) -> p e r", e=E),
                                         in0=side_ps[slot][:, 0:RANKS].rearrange("p (e r) -> p e r", e=E),
                                         scalar=weight[:, 0:1],
                                         in1=route[:, :].unsqueeze(2).to_broadcast([P, E, R]),
                                         op0=ALU.mult, op1=ALU.mult).then_inc(hw_ready, 1)

            def low_hwT(t, slot):
                dve.wait_ge(hwT_hi_ready, t + 1)
                dve.tensor_tensor(hwT_lo[slot][:, :], hwT_ps[slot][:, 0:P], hwT_hi[slot][:, :].bitcast(f32),
                                  ALU.subtract).then_inc(hwT_lo_ready, 1)

            def finish(t, slot):
                dve.wait_ge(base_done, t + 1)
                dve.wait_ge(xb_ready, t + 1)
                dve.tensor_tensor(cols(xb_all, t), base_ps[slot][:, :], cols(xb_all, t), ALU.add)\
                    .then_inc(result_ready, 1)

            dve.wait_ge(mask_ready, 1)
            select(0, 0, 0)
            select(1, 1, 0)
            for c in range(CHUNKS):
                low_w(c)
            low_y(0, 0)
            dve.wait_ge(b_hi_ready, 1)
            dve.tensor_tensor(b_lo[:, :], b_raw[:, :], b_hi[:, :].bitcast(f32), ALU.subtract)\
                .then_inc(b_lo_ready, 1)
            dve.wait_ge(experts_ready, 1)

            def step(t, slot, pair):
                if at_least(t, 1):
                    route_tile(t - 1, 1 - slot)
                if exists(t, 2):
                    select(t + 2, slot, pair + 1)
                if at_least(t, 1):
                    low_hwT(t - 1, 1 - slot)
                if exists(t, 1):
                    low_y(t + 1, 1 - slot)
                if at_least(t, 1):
                    finish(t - 1, 1 - slot)
            over_tiles(dve, step)
            route_tile(TILES - 1, 1)
            low_hwT(TILES - 1, 1)
            finish(TILES - 1, 1)

        @block.tensor
        def _(pe):
            def mix_tile(t, slot):
                pe.wait_ge(mix_ready, t + 1)
                pe.wait_ge(x_lo_ready, t + 1)
                if at_least(t, 2):
                    pe.wait_ge(y_lo_ready, t - 1)
                m_hi, m_lo = mix[slot][:, 0, :], mix[slot][:, 1, :]
                for c in range(CHUNKS):
                    f = slice(c * P, (c + 1) * P)
                    dst = y_ps[slot][:, f]
                    pe.matmul(dst, x_hi[slot][:, f], m_hi, start=True, stop=False)
                    pe.matmul(dst, x_hi[slot][:, f], m_lo, start=False, stop=False)
                    last = pe.matmul(dst, x_lo[slot][:, f], m_hi, start=False, stop=True)
                last.then_inc(y_done, 1)

            def main_chunk(t, slot, c):
                if not at_least(t, 1):
                    pe.wait_ge(w_lo_ready, c + 1)
                f = slice(c * P, (c + 1) * P)
                first, final = c == 0, c == CHUNKS - 1
                base, side = base_ps[slot][:, :], side_ps[slot][:, 0:SIDE]
                for n, (y, w) in enumerate(((y_hi, w_hi), (y_hi, w_lo), (y_lo, w_hi))):
                    pe.matmul(base, y[slot][:, f], w[:, c, 0:OUT], start=first and n == 0, stop=False)
                    last = pe.matmul(side, y[slot][:, f], w[:, c, OUT:ALL],
                                     start=first and n == 0, stop=final and n == 2)
                if final:
                    last.then_inc(main_done, 1)

            def turn(t, slot):
                pe.wait_ge(hw_ready, t + 1)
                if at_least(t, 2):
                    pe.wait_ge(hwT_lo_ready, t - 1)
                pe.transpose(hwT_ps[slot][:, 0:P], hw[slot][:, :], ident[:, :]).then_inc(hwT_done, 1)

            def lora(t, slot):
                pe.wait_ge(hwT_lo_ready, t + 1)
                dst = base_ps[slot][:, :]
                pe.matmul(dst, hwT_hi[slot][:, :], b_hi[:, :], start=False, stop=False)
                pe.matmul(dst, hwT_hi[slot][:, :], b_lo[:, :], start=False, stop=False)
                pe.matmul(dst, hwT_lo[slot][:, :], b_hi[:, :], start=False, stop=True)\
                    .then_inc(base_done, 1)

            mix_tile(0, 0)
            pe.wait_ge(ident_ready, 1)

            def step(t, slot, pair):
                if exists(t, 1):
                    mix_tile(t + 1, 1 - slot)
                pe.wait_ge(y_lo_ready, t + 1)
                if at_least(t, 2):
                    pe.wait_ge(result_ready, t - 1)
                    pe.wait_ge(hw_ready, t - 1)
                main_chunk(t, slot, 0)
                main_chunk(t, slot, 1)
                if at_least(t, 1):
                    turn(t - 1, 1 - slot)
                main_chunk(t, slot, 2)
                if at_least(t, 1):
                    if not at_least(t, 2):
                        pe.wait_ge(b_lo_ready, 1)
                    lora(t - 1, 1 - slot)
                main_chunk(t, slot, 3)
            over_tiles(pe, step)
            turn(TILES - 1, 1)
            lora(TILES - 1, 1)


def kernel(**inputs):
    import numpy as np
    import concourse.bacc as bacc
    from concourse import mybir as mb
    from concourse.bass_utils import run_bass_kernel_spmd as run

    batches, channels, features = inputs["x"].shape
    quarter = 128 // channels
    ranks = inputs["L0_ffn_A"].shape[0] * inputs["L0_ffn_A"].shape[1]
    arrays = {
        "x": inputs["x"],
        "cond": inputs["itok_B_0_15"].reshape(-1, quarter).T,
        "cond_w": inputs["L0_cond_weights"].reshape(-1, channels),
        "w_all": np.concatenate([np.asarray(inputs["L0_ffn_W_base"]),
                                 np.asarray(inputs["L0_ffn_A"]).reshape(ranks, features),
                                 np.asarray(inputs["L0_ffn_W_gate"])], axis=0).T,
        "b_lora": np.asarray(inputs["L0_ffn_B"]).transpose(0, 2, 1).reshape(ranks, -1),
        "bias": inputs["L0_ffn_b_base"].reshape(1, -1),
    }
    arrays = {name: np.ascontiguousarray(a) for name, a in arrays.items()}
    nc = bacc.Bacc("TRN2", target_bir_lowering=False, num_devices=1)
    args = [nc.dram_tensor(name, a.shape, mb.dt.from_np(a.dtype), kind="ExternalInput").ap()
            for name, a in arrays.items()]
    out = nc.dram_tensor("out", (batches, channels, features), mb.dt.float32, kind="ExternalOutput").ap()
    adaln_ffn_kernel(nc, *args, out)
    r = run(nc, [arrays], core_ids=[0])
    return r.results[0]["out"]
```

```python
import concourse.bass as bass
from concourse import mybir
from contextlib import ExitStack


def adaln_ffn_kernel(
    nc: bass.Bass,
    x: bass.AP,
    cond: bass.AP,
    cond_w: bass.AP,
    w_all: bass.AP,
    b_lora: bass.AP,
    bias: bass.AP,
    out: bass.AP,
):
    f32 = mybir.dt.float32
    f32r = mybir.dt.float32r
    i32 = mybir.dt.int32
    u32 = mybir.dt.uint32
    ALU = mybir.AluOpType
    ACT = mybir.ActivationFunctionType

    P = 128
    BATCHES, C, D = x.shape
    Q = P // C
    TILES = BATCHES // Q
    CHUNKS = D // P
    RANKS = b_lora.shape[0]
    E = w_all.shape[1] - D - RANKS
    R = RANKS // E
    OUT = D
    BASE, H, G = OUT // 2, RANKS // 2, E // 2
    HALF = BASE + H
    ALL = 2 * HALF + E
    SIDE = H + E
    PAIRS = TILES // 2
    LAST = TILES - 1
    ORDER = [(c, n) for c in range(CHUNKS) for n in range(3)]
    FIRST_ORDER = [(0, 0), (0, 1), (1, 0), (1, 1), (0, 2), (1, 2)] + ORDER[6:]
    STEPS = len(ORDER)
    TURN_AT, LORA_AT = 4, 9
    LAST_TURN_AT = 1, 7
    WARM_UP = 14

    x_tiles = x.rearrange("(t q) c n -> t (q c) n", q=Q)
    out_tiles = out.rearrange("(t q) c n -> t (q c) n", q=Q)
    w_chunks = w_all.rearrange("(c p) n -> c p n", p=P)

    ctx = ExitStack()
    with ctx:
        def sb(name, shape, dt=f32):
            return ctx.enter_context(nc.sbuf_tensor(name, shape, dt))

        def ps(name):
            return ctx.enter_context(nc.psum_tensor(name, [P, 512], f32))

        def sem(name):
            return ctx.enter_context(nc.semaphore(name))

        x_in = [sb(f"x_in{i}", [P, D]) for i in range(2)]
        xb_all = sb("xb_all", [P, TILES * D])
        w_raw = sb("w_raw", [P, CHUNKS, ALL])
        w_hi = sb("w_hi", [P, CHUNKS, ALL], f32r)
        w_lo = sb("w_lo", [P, CHUNKS, ALL], f32r)
        b_raw = sb("b_raw", [P, OUT])
        b_hi = sb("b_hi", [P, OUT], f32r)
        b_lo = sb("b_lo", [P, OUT], f32r)
        bias_sb = sb("bias_sb", [P, OUT])
        warm = sb("warm", [P, 512], mybir.dt.bfloat16)
        ident = sb("ident", [P, P])
        diag_mask = sb("diag_mask", [P, Q, C])
        channel = sb("channel", [P, 1], i32)
        expert_ids = sb("expert_ids", [P, E])
        cond_sb = sb("cond_sb", [P, TILES], i32)
        row_ids = sb("row_ids", [P, TILES], i32)
        row_now = [sb(f"row_now{i}", [P, 1], i32) for i in range(2)]
        mixw = [sb(f"mixw{i}", [P, C]) for i in range(2)]
        mix = [sb(f"mix{i}", [P, Q, C]) for i in range(2)]
        y_hi = [sb(f"y_hi{i}", [P, D], f32r) for i in range(2)]
        y_lo = [sb(f"y_lo{i}", [P, D], f32r) for i in range(2)]
        hw = [sb(f"hw{i}", [P, RANKS]) for i in range(2)]
        hwT_hi = [sb(f"hwT_hi{i}", [P, P], f32r) for i in range(2)]
        hwT_lo = [sb(f"hwT_lo{i}", [P, P], f32r) for i in range(2)]
        top = sb("top", [P, 8])
        top_ids = sb("top_ids", [P, 8], u32)
        one_hot = sb("one_hot", [P, 2, E])
        second = sb("second", [P, 1])
        total = sb("total", [P, 1])
        weight = sb("weight", [P, 1])
        route = sb("route", [P, E])

        y_ps = [ps(f"y_ps{i}") for i in range(2)]
        main_ps = [ctx.enter_context(nc.psum_tensor(f"main_ps{i}", [P, 2, 512], f32)) for i in range(2)]
        hwT_ps = [ps(f"hwT_ps{i}") for i in range(2)]

        x_landed = [sem(f"x_landed{i}") for i in range(2)]
        cond_landed = sem("cond_landed")
        w_landed = [sem(f"w_landed{c}") for c in range(CHUNKS)]
        b_landed = sem("b_landed")
        bias_landed = sem("bias_landed")
        mixw_landed = [sem(f"mixw_landed{i}") for i in range(2)]
        warm_ready = sem("warm_ready")
        channel_ready = sem("channel_ready")
        cleared = sem("cleared")
        mask_ready = sem("mask_ready")
        experts_ready = sem("experts_ready")
        ident_ready = sem("ident_ready")
        rows_ready = sem("rows_ready")
        row_staged = sem("row_staged")
        mix_ready = sem("mix_ready")
        xb_ready = sem("xb_ready")
        w_hi_ready = sem("w_hi_ready")
        w_lo_ready = sem("w_lo_ready")
        b_hi_ready = sem("b_hi_ready")
        b_lo_ready = sem("b_lo_ready")
        first_y_done = sem("first_y_done")
        first_y_hi_ready = sem("first_y_hi_ready")
        first_y_lo_ready = sem("first_y_lo_ready")
        y_done = sem("y_done")
        y_hi_ready = sem("y_hi_ready")
        y_lo_ready = sem("y_lo_ready")
        main_done = sem("main_done")
        top_ready = sem("top_ready")
        ids_ready = sem("ids_ready")
        one_hot_ready = sem("one_hot_ready")
        second_ready = sem("second_ready")
        total_ready = sem("total_ready")
        weight_ready = sem("weight_ready")
        hw_ready = sem("hw_ready")
        hwT_done = sem("hwT_done")
        hwT_hi_ready = sem("hwT_hi_ready")
        hwT_lo_ready = sem("hwT_lo_ready")
        base_done = sem("base_done")
        result_ready = sem("result_ready")
        stored = sem("stored")

        def cols(buf, t):
            return buf[:, bass.ds(t * D, D)]

        def over_tiles(eng, step):
            for slot in range(2):
                step(slot, slot, 0)
            with eng.Fori(1, PAIRS - 1) as pair:
                for slot in range(2):
                    step(pair * 2 + slot, slot, pair)
            for slot in range(2):
                step(TILES - 2 + slot, slot, PAIRS - 1)

        def known(t):
            return isinstance(t, int)

        def held(eng, value):
            return value if known(value) else eng.to_reg(value)

        def at_least(t, n):
            return t >= n if known(t) else True

        def exists(t, ahead):
            return t + ahead < TILES if known(t) else True

        def first_halves():
            for h, bank in enumerate((y_ps[0], hwT_ps[0])):
                f = slice(h * D // 2, (h + 1) * D // 2)
                yield bank[:, 0:D // 2], y_hi[0][:, f], y_lo[0][:, f]

        block = ctx.enter_context(nc.Block())

        @block.sync
        def _(sp):
            def load_x(t, slot, pair):
                if at_least(t, 2):
                    sp.wait_ge(y_done, t - 1)
                    sp.wait_ge(xb_ready, t - 1)
                sp.dma_start(x_in[slot][:, :], x_tiles[t, :, :]).then_inc(x_landed[slot], 16)

            def load_w(c):
                sp.dma_start(w_raw[:, c, :], w_chunks[c, :, :]).then_inc(w_landed[c], 16)

            def store(t, slot, pair):
                sp.wait_ge(result_ready, t + 1)
                sp.dma_start(out_tiles[t, :, :], cols(xb_all, t)).then_inc(stored, 16)

            sp.dma_start(cond_sb[:, :], cond).then_inc(cond_landed, 16)
            load_x(0, 0, 0)
            load_w(0)
            sp.wait_ge(rows_ready, 1)
            load_w(1)
            load_x(1, 1, 0)
            load_w(2)
            sp.dma_start(bias_sb[:, :], bias.to_broadcast([P, OUT])).then_inc(bias_landed, 16)
            load_w(3)
            sp.dma_start(b_raw[:, :], b_lora).then_inc(b_landed, 16)

            LEAD = 4
            for t in range(2, LEAD):
                load_x(t, t % 2, t // 2)
            with sp.Fori(0, (TILES - LEAD) // 2) as pair:
                for slot in range(2):
                    load_x(pair * 2 + LEAD + slot, slot, pair + LEAD // 2)
                    store(pair * 2 + slot, slot, pair)
            for t in range(TILES - LEAD, LAST):
                store(t, t % 2, t // 2)
            for half in range(2):
                n = slice(half * BASE, (half + 1) * BASE)
                sp.wait_ge(result_ready, LAST + half + 1)
                sp.dma_start(out_tiles[LAST, :, n], cols(xb_all, LAST)[:, n]).then_inc(stored, 16)
            sp.wait_ge(stored, 16 * (TILES + 1))

        @block.gpsimd
        def _(pool):
            for q in range(Q):
                last = pool.iota(channel[q * C:(q + 1) * C, :], [[0, 1]], base=0, channel_multiplier=1)
            last.then_inc(channel_ready, 1)

            def gather(t, slot):
                if known(t):
                    ids = row_ids[:, t:t + 1]
                    if t >= 2:
                        pool.wait_ge(mix_ready, t - 1)
                else:
                    ids = row_now[slot][:, :]
                    count = held(pool, t - 3)
                    pool.wait_ge(mix_ready, t - 1)
                    pool.tensor_copy(ids, row_ids[:, bass.ds(t, 1)]).then_inc(row_staged, 1)
                    pool.wait_ge(rows_ready, 1)
                    pool.wait_ge(row_staged, count)
                pool.indirect_dma_start(mixw[slot][:, :], None, cond_w,
                                        bass.IndirectOffsetOnAxis(ids, 0))\
                    .then_inc(mixw_landed[slot], 16)

            pool.wait_ge(rows_ready, 1)
            gather(0, 0)
            gather(1, 1)
            pool.memset(diag_mask[:, :, :], 0.0).then_inc(cleared, 1)
            pool.memset(ident[:, :], 0.0).then_inc(cleared, 1)
            pool.wait_ge(cleared, 2)
            for q in range(Q):
                last = pool.memset(diag_mask[q * C:(q + 1) * C, q, :], 1.0)
            last.then_inc(mask_ready, 1)
            pool.wait_ge(mask_ready, 1)
            pool.affine_select(out=ident[:, :], in_=ident[:, :], compare_op=ALU.not_equal, fill=1.0,
                               base=0, pattern=[[-1, P]], channel_multiplier=1).then_inc(ident_ready, 1)
            pool.wait_ge(ident_ready, 1)
            pool.iota(expert_ids[:, :], [[1, E]], base=0, channel_multiplier=0,
                      allow_small_or_imprecise_dtypes=True).then_inc(experts_ready, 1)

            gather(2, 0)

            def prepare(t, slot, pair):
                if not at_least(t, 1):
                    pool.wait_ge(bias_landed, 16)
                pool.wait_ge(x_landed[slot], pair * 16 + 16)
                pool.tensor_tensor(cols(xb_all, t), x_in[slot][:, :], bias_sb[:, :], ALU.add)\
                    .then_inc(xb_ready, 1)
                if at_least(t, 1) and exists(t, 2):
                    gather(t + 2, slot)
            over_tiles(pool, prepare)

        @block.scalar
        def _(act):
            def split_w(c):
                act.wait_ge(w_landed[c], 16)
                act.activation(w_hi[:, c, :], w_raw[:, c, :], ACT.Copy).then_inc(w_hi_ready, 1)

            def split_y(t, slot):
                act.wait_ge(y_done, t + 1)
                if at_least(t, 2):
                    act.wait_ge(main_done, t - 1)
                act.activation(y_hi[slot][:, :], y_ps[slot][:, :], ACT.Copy).then_inc(y_hi_ready, 1)

            def exp_second(t):
                act.wait_ge(top_ready, t + 1)
                act.activation(second[:, :], top[:, 0:1], ACT.Exp, bias=top[:, 1:2], scale=-1.0)\
                    .then_inc(second_ready, 1)

            def split_hwT(t, slot):
                act.wait_ge(hwT_done, t + 1)
                if at_least(t, 2):
                    act.wait_ge(base_done, t - 1)
                act.activation(hwT_hi[slot][:, :], hwT_ps[slot][:, 0:P], ACT.Copy)\
                    .then_inc(hwT_hi_ready, 1)

            split_w(0)
            split_w(1)
            for (y, hi, _), done, ready in zip(first_halves(), (first_y_done, y_done),
                                               (first_y_hi_ready, y_hi_ready)):
                act.wait_ge(done, 1)
                act.activation(hi, y, ACT.Copy).then_inc(ready, 1)
            split_w(2)
            split_w(3)
            act.wait_ge(b_landed, 16)
            act.activation(b_hi[:, :], b_raw[:, :], ACT.Copy).then_inc(b_hi_ready, 1)

            def step(t, slot, pair):
                if at_least(t, 1):
                    exp_second(t - 1)
                if known(t) and t == LAST:
                    exp_second(LAST)
                if exists(t, 1):
                    split_y(t + 1, 1 - slot)
                if at_least(t, 1):
                    split_hwT(t - 1, 1 - slot)
            over_tiles(act, step)
            split_hwT(LAST, 1)

        @block.vector
        def _(dve):
            dve.memset(warm[:, :], 0.0).then_inc(warm_ready, 1)
            dve.wait_ge(cond_landed, 16)
            dve.wait_ge(channel_ready, 1)
            dve.scalar_tensor_tensor(out=row_ids[:, :], in0=cond_sb[:, :], scalar=float(C),
                                     in1=channel[:, 0:1].to_broadcast([P, TILES]),
                                     op0=ALU.mult, op1=ALU.add).then_inc(rows_ready, 1)

            def select(t, slot, pair):
                dve.wait_ge(mixw_landed[slot], pair * 16 + 16)
                dve.tensor_tensor(mix[slot][:, :, :], mixw[slot][:, :].unsqueeze(1).to_broadcast([P, Q, C]),
                                  diag_mask[:, :, :], ALU.mult).then_inc(mix_ready, 1)

            def low_w(c):
                dve.wait_ge(w_hi_ready, c + 1)
                dve.tensor_tensor(w_lo[:, c, :], w_raw[:, c, :], w_hi[:, c, :].bitcast(f32),
                                  ALU.subtract).then_inc(w_lo_ready, 1)

            def low_y(t, slot):
                dve.wait_ge(y_hi_ready, t + 1)
                dve.tensor_tensor(y_lo[slot][:, :], y_ps[slot][:, :], y_hi[slot][:, :].bitcast(f32),
                                  ALU.subtract).then_inc(y_lo_ready, 1)

            def route_tile(t, slot, h=None, logits=None):
                if h is None:
                    h, logits = main_ps[slot][:, :, BASE:HALF], main_ps[slot][:, 1, HALF:HALF + E]
                count = held(dve, t + 1)
                dve.wait_ge(experts_ready, 1)
                dve.wait_ge(main_done, count)
                dve.max(top[:, :], logits).then_inc(top_ready, 1)
                dve.wait_ge(experts_ready, 1)
                dve.wait_ge(top_ready, count)
                dve.max_index(top_ids[:, :], top[:, :], logits).then_inc(ids_ready, 1)
                dve.wait_ge(ids_ready, t + 1)
                dve.tensor_tensor(one_hot[:, :, :],
                                  expert_ids[:, :].unsqueeze(1).to_broadcast([P, 2, E]),
                                  top_ids[:, 0:2].unsqueeze(2).to_broadcast([P, 2, E]),
                                  ALU.is_equal).then_inc(one_hot_ready, 1)
                dve.wait_ge(second_ready, t + 1)
                dve.tensor_scalar(total[:, :], second[:, :], 1.0, None, ALU.add).then_inc(total_ready, 1)
                dve.wait_ge(one_hot_ready, t + 1)
                if at_least(t, 1):
                    dve.wait_ge(hw_ready, t)
                dve.scalar_tensor_tensor(out=route[:, :], in0=one_hot[:, 1, :], scalar=second[:, 0:1],
                                         in1=one_hot[:, 0, :], op0=ALU.mult, op1=ALU.add)
                dve.wait_ge(total_ready, t + 1)
                dve.reciprocal(weight[:, :], total[:, :]).then_inc(weight_ready, 1)
                dve.wait_ge(weight_ready, t + 1)
                dve.scalar_tensor_tensor(
                    out=hw[slot][:, :].rearrange("p (h e r) -> p h e r", h=2, e=G),
                    in0=h.rearrange("p h (e r) -> p h e r", e=G),
                    scalar=weight[:, 0:1],
                    in1=route[:, :].rearrange("p (h e) -> p h e", h=2).unsqueeze(3).to_broadcast([P, 2, G, R]),
                    op0=ALU.mult, op1=ALU.mult).then_inc(hw_ready, 1)

            def low_hwT(t, slot):
                dve.wait_ge(hwT_hi_ready, t + 1)
                dve.tensor_tensor(hwT_lo[slot][:, :], hwT_ps[slot][:, 0:P], hwT_hi[slot][:, :].bitcast(f32),
                                  ALU.subtract).then_inc(hwT_lo_ready, 1)

            def finish(t, slot):
                dve.wait_ge(base_done, t + 1)
                dve.wait_ge(xb_ready, t + 1)
                tile = cols(xb_all, t).rearrange("p (h n) -> p h n", h=2)
                dve.tensor_tensor(tile, main_ps[slot][:, :, 0:BASE], tile, ALU.add)\
                    .then_inc(result_ready, 1)

            low_w(0)
            dve.wait_ge(mask_ready, 1)
            select(0, 0, 0)
            low_w(1)
            for (y, hi, lo), have, ready in zip(first_halves(), (first_y_hi_ready, y_hi_ready),
                                                (first_y_lo_ready, y_lo_ready)):
                dve.wait_ge(have, 1)
                dve.tensor_tensor(lo, y, hi.bitcast(f32), ALU.subtract).then_inc(ready, 1)
            select(1, 1, 0)
            low_w(2)
            low_w(3)
            dve.wait_ge(b_hi_ready, 1)
            dve.tensor_tensor(b_lo[:, :], b_raw[:, :], b_hi[:, :].bitcast(f32), ALU.subtract)\
                .then_inc(b_lo_ready, 1)
            dve.wait_ge(experts_ready, 1)

            def step(t, slot, pair):
                if at_least(t, 1):
                    route_tile(t - 1, 1 - slot)
                if exists(t, 2):
                    select(t + 2, slot, pair + 1)
                last = known(t) and t == LAST
                if last:
                    side = y_ps[0][:, 0:2 * SIDE].rearrange("p (h n) -> p h n", h=2)
                    route_tile(LAST, 1, side[:, :, 0:H], side[:, 1, H:SIDE])
                if at_least(t, 1):
                    low_hwT(t - 1, 1 - slot)
                if exists(t, 1):
                    low_y(t + 1, 1 - slot)
                if last:
                    low_hwT(LAST, 1)
                if at_least(t, 1):
                    finish(t - 1, 1 - slot)
            over_tiles(dve, step)
            dve.wait_ge(xb_ready, TILES)
            for half in range(2):
                n = slice(half * BASE, (half + 1) * BASE)
                dve.wait_ge(base_done, LAST + half + 1)
                dve.tensor_tensor(cols(xb_all, LAST)[:, n], main_ps[1][:, half, 0:BASE],
                                  cols(xb_all, LAST)[:, n], ALU.add).then_inc(result_ready, 1)

        @block.tensor
        def _(pe):
            def mix_tile(t, slot, pair):
                pe.wait_ge(mix_ready, t + 1)
                pe.wait_ge(x_landed[slot], pair * 16 + 16)
                if at_least(t, 2):
                    pe.wait_ge(y_lo_ready, t - 1)
                for c in range(CHUNKS):
                    f = slice(c * P, (c + 1) * P)
                    dst = y_ps[slot][:, f]
                    if not at_least(t, 1) and c >= CHUNKS // 2:
                        dst = hwT_ps[0][:, (c - CHUNKS // 2) * P:(c - CHUNKS // 2 + 1) * P]
                    last = pe.matmul(dst, x_in[slot][:, f], mix[slot][:, :, :], start=True, stop=True)
                    if not at_least(t, 1) and c == CHUNKS // 2 - 1:
                        last.then_inc(first_y_done, 1)
                last.then_inc(y_done, 1)

            def operands(c, n, slot):
                y, w = ((y_hi, w_hi), (y_hi, w_lo), (y_lo, w_hi))[n]
                return y[slot][:, c * P:(c + 1) * P], w[:, c, :]

            def side_columns(w):
                first = w[:, BASE:BASE + SIDE]
                return bass.AP(first.tensor, first.offset, [first.ap[0], [HALF, 2], [1, SIDE]])

            def main(t, slot, steps):
                for i in steps:
                    c, n = (FIRST_ORDER if not at_least(t, 1) else ORDER)[i]
                    if not at_least(t, 1):
                        if n == 0:
                            pe.wait_ge(w_hi_ready, c + 1)
                        if n == 1:
                            pe.wait_ge(w_lo_ready, c + 1)
                        if i == 0:
                            pe.wait_ge(first_y_hi_ready, 1)
                        if (c, n) == (0, 2):
                            pe.wait_ge(first_y_lo_ready, 1)
                        if (c, n) == (CHUNKS // 2, 0):
                            pe.wait_ge(y_lo_ready, 1)
                    y, w = operands(c, n, slot)
                    for half in range(2):
                        n_cols = HALF + half * E
                        last = pe.matmul(main_ps[slot][:, half, 0:n_cols], y,
                                         w[:, half * HALF:half * HALF + n_cols],
                                         start=i == 0, stop=i == STEPS - 1)
                if i == STEPS - 1:
                    last.then_inc(main_done, 1)

            def turn(t, slot):
                pe.wait_ge(hw_ready, t + 1)
                if at_least(t, 2):
                    pe.wait_ge(hwT_lo_ready, t - 1)
                pe.transpose(hwT_ps[slot][:, 0:P], hw[slot][:, :], ident[:, :]).then_inc(hwT_done, 1)

            def lora(t, slot, by_half=False):
                pe.wait_ge(hwT_lo_ready, t + 1)
                parts = ((hwT_hi, b_hi), (hwT_hi, b_lo), (hwT_lo, b_hi))
                order = [(n, half) for n in range(3) for half in range(2)]
                if by_half:
                    order.sort(key=lambda x: x[1])
                for n, half in order:
                    h, w = parts[n]
                    last = pe.matmul(main_ps[slot][:, half, 0:BASE], h[slot][:, :],
                                     w[:, half * BASE:(half + 1) * BASE],
                                     start=False, stop=n == 2, skip_group_check=True)
                    if (n, half) == order[-1] or by_half and n == 2:
                        last.then_inc(base_done, 1)

            pe.wait_ge(warm_ready, 1)
            for _ in range(WARM_UP):
                pe.matmul(hwT_ps[1][:, :], warm[:, 0:P], warm[:, :], start=True, stop=True)

            mix_tile(0, 0, 0)
            pe.wait_ge(ident_ready, 1)

            def begin(t, slot, pair):
                if not at_least(t, 1):
                    return
                if exists(t, 1):
                    mix_tile(t + 1, 1 - slot, pair + slot)
                pe.wait_ge(y_lo_ready, t + 1)
                if at_least(t, 2):
                    pe.wait_ge(result_ready, t - 1)

            def step(t, slot, pair):
                if known(t) and t == LAST:
                    return
                begin(t, slot, pair)
                main(t, slot, range(0, TURN_AT))
                if at_least(t, 1):
                    turn(t - 1, 1 - slot)
                else:
                    mix_tile(1, 1, 0)
                main(t, slot, range(TURN_AT, LORA_AT))
                if at_least(t, 1):
                    if not at_least(t, 2):
                        pe.wait_ge(b_lo_ready, 1)
                    lora(t - 1, 1 - slot)
                main(t, slot, range(LORA_AT, STEPS))
            over_tiles(pe, step)

            pe.wait_ge(y_lo_ready, TILES)
            side = y_ps[0][:, 0:2 * SIDE].rearrange("p (h n) -> p h n", h=2)
            for i in range(STEPS):
                y, w = operands(*ORDER[i], 1)
                last = pe.matmul(side, y, side_columns(w), start=i == 0, stop=i == STEPS - 1)
            last.then_inc(main_done, 1)
            pe.wait_ge(result_ready, LAST - 1)
            for i in range(STEPS):
                y, w = operands(*ORDER[i], 1)
                for half in range(2):
                    pe.matmul(main_ps[1][:, half, 0:BASE], y, w[:, half * HALF:half * HALF + BASE],
                              start=i == 0, stop=i == STEPS - 1)
                if i == LAST_TURN_AT[0]:
                    turn(LAST - 1, 0)
                if i == LAST_TURN_AT[1]:
                    turn(LAST, 1)
                    lora(LAST - 1, 0)
            lora(LAST, 1, by_half=True)


def kernel(**inputs):
    import numpy as np
    import concourse.bacc as bacc
    from concourse import mybir as mb
    from concourse.bass_utils import run_bass_kernel_spmd as run

    batches, channels, features = inputs["x"].shape
    quarter = 128 // channels
    ranks = inputs["L0_ffn_A"].shape[0] * inputs["L0_ffn_A"].shape[1]
    half_out, half_e = features // 2, inputs["L0_ffn_A"].shape[0] // 2
    base, gate = np.asarray(inputs["L0_ffn_W_base"]), np.asarray(inputs["L0_ffn_W_gate"])
    down, up = np.asarray(inputs["L0_ffn_A"]), np.asarray(inputs["L0_ffn_B"])
    columns = []
    for h in range(2):
        experts = slice(h * half_e, (h + 1) * half_e)
        columns += [base[h * half_out:(h + 1) * half_out], down[experts].reshape(-1, features)]
    arrays = {
        "x": inputs["x"],
        "cond": np.repeat(np.asarray(inputs["itok_B_0_15"]).reshape(-1, quarter).T, channels, axis=0),
        "cond_w": inputs["L0_cond_weights"].reshape(-1, channels),
        "w_all": np.concatenate(columns + [gate], axis=0).T,
        "b_lora": up.transpose(0, 2, 1).reshape(ranks, -1),
        "bias": inputs["L0_ffn_b_base"].reshape(1, -1),
    }
    arrays = {name: np.ascontiguousarray(a) for name, a in arrays.items()}
    nc = bacc.Bacc("TRN2", target_bir_lowering=False, num_devices=1)
    args = [nc.dram_tensor(name, a.shape, mb.dt.from_np(a.dtype), kind="ExternalInput").ap()
            for name, a in arrays.items()]
    out = nc.dram_tensor("out", (batches, channels, features), mb.dt.float32, kind="ExternalOutput").ap()
    adaln_ffn_kernel(nc, *args, out)
    r = run(nc, [arrays], core_ids=[0])
    return r.results[0]["out"]
```
